# Optimizing a Trainium2 kernel written in Bass

```python
import numpy as np
import jax
import jax.numpy as jnp

def _softmax(x, axis=-1):
    return jax.nn.softmax(x, axis=axis)

def _gelu(x):
    return jax.nn.gelu(x, approximate=True)

def _silu(x):
    return jax.nn.silu(x)

def _sigmoid(x):
    return jax.nn.sigmoid(x)

def _layernorm(x, axis=-1, eps=1e-05):
    m = jnp.mean(x, axis=axis, keepdims=True)
    v = jnp.var(x, axis=axis, keepdims=True)
    return (x - m) / jnp.sqrt(v + eps)

def _scatter_add(tgt, idx, src, axis=0):
    return tgt.at[idx].add(src)

def _segment_sum(src, seg, n):
    return jax.ops.segment_sum(src, seg, n)
kernel_name = 'mk_cond_resid_d2_seqx_r4_89a3e4'

def setup_inputs(seed: int=0):
    np.random.seed(seed)
    _w = jnp.asarray

    def _rec_inputs():
        import jax
        import jax.numpy as jnp
        _rk = jax.random.key(seed)
        x = 7.22e-05 + 1 * jax.random.normal(jax.random.fold_in(_rk, 1), (8, 256, 256), jnp.float32)
        _lenS = 256 - jax.random.randint(jax.random.fold_in(_rk, 7), (8,), 0, max(1, 256 // 4) + 1, jnp.int32)
        _lenS2 = 256 - jax.random.randint(jax.random.fold_in(_rk, 8), (8,), 0, max(1, 256 // 4) + 1, jnp.int32)
        fside_BxSxS_0 = 4.13588e-05 + 0.999923 * jax.random.normal(jax.random.fold_in(_rk, 11), (8, 256, 256), jnp.float32)
        itok_B_0_5 = jax.random.randint(jax.random.fold_in(_rk, 12), (8,), 0, 6, jnp.int32)
        fside_Bx8_0 = jax.random.uniform(jax.random.fold_in(_rk, 13), (8, 8), jnp.float32, 0.0, 0.556406)
        condB_sharedgateprob = jax.random.uniform(jax.random.fold_in(_rk, 14), (8,), jnp.float32, 0.0, 0.794948)
        return (x, fside_BxSxS_0, itok_B_0_5, fside_Bx8_0, condB_sharedgateprob)
    x, fside_BxSxS_0, itok_B_0_5, fside_Bx8_0, condB_sharedgateprob = _rec_inputs()

    def _L0_cond_setup():
        import jax, jax.numpy as jnp
        import numpy as np
        B, S, D = (8, 256, 256)
        NUM_STAGES = 6
        key = jax.random.key(seed)
        k1, k2, k3, k4, k5 = jax.random.split(key, 5)
        return {'query': jax.random.normal(k1, (B, S, D), dtype=jnp.float32), 'key': jax.random.normal(k2, (B, S, D), dtype=jnp.float32), 'value': jax.random.normal(k3, (B, S, D), dtype=jnp.float32), 'braak_embed': jax.random.normal(k4, (NUM_STAGES, D), dtype=jnp.float32), 'braak_stages': jax.random.randint(k5, (B,), 0, NUM_STAGES, dtype=jnp.int64)}
    _L0_cond_all = _L0_cond_setup()
    _L0_cond_in = {k: v for k, v in _L0_cond_all.items() if k in ('braak_embed',)}
    del _L0_cond_all

    def _L1_cond_setup():
        import jax, jax.numpy as jnp
        import numpy as np
        E, B, S, D, F = (8, 2, 256, 256, 1024)
        key = jax.random.key(seed)
        ks = jax.random.split(key, 9)
        sc_d = 1.0 / np.sqrt(D)
        sc_f = 1.0 / np.sqrt(F)
        hidden_states = jax.random.normal(ks[0], (B, S, D), dtype=jnp.float32)
        gating_probs = jax.nn.softmax(jax.random.normal(ks[1], (B, E), dtype=jnp.float32), axis=-1)
        shared_gate_prob = jax.nn.sigmoid(jax.random.normal(ks[2], (B, 1), dtype=jnp.float32))
        Wg = jax.random.normal(ks[3], (E, D, F), dtype=jnp.float32) * sc_d
        Wu = jax.random.normal(ks[4], (E, D, F), dtype=jnp.float32) * sc_d
        Wd = jax.random.normal(ks[5], (E, F, D), dtype=jnp.float32) * sc_f
        Sg = jax.random.normal(ks[6], (D, F), dtype=jnp.float32) * sc_d
        Su = jax.random.normal(ks[7], (D, F), dtype=jnp.float32) * sc_d
        Sd = jax.random.normal(ks[8], (F, D), dtype=jnp.float32) * sc_f
        return {'hidden_states': hidden_states, 'gating_probs': gating_probs, 'shared_gate_prob': shared_gate_prob, 'Wg': Wg, 'Wu': Wu, 'Wd': Wd, 'Sg': Sg, 'Su': Su, 'Sd': Sd}
    _L1_cond_all = _L1_cond_setup()
    _L1_cond_in = {k: v for k, v in _L1_cond_all.items() if k in ('Wg', 'Wu', 'Wd', 'Sg', 'Su', 'Sd')}
    del _L1_cond_all
    return {'x': x, 'fside_BxSxS_0': fside_BxSxS_0, 'itok_B_0_5': itok_B_0_5, 'fside_Bx8_0': fside_Bx8_0, 'condB_sharedgateprob': condB_sharedgateprob, 'L0_cond_braak_embed': _L0_cond_in['braak_embed'], 'L1_cond_Wg': _L1_cond_in['Wg'], 'L1_cond_Wu': _L1_cond_in['Wu'], 'L1_cond_Wd': _L1_cond_in['Wd'], 'L1_cond_Sg': _L1_cond_in['Sg'], 'L1_cond_Su': _L1_cond_in['Su'], 'L1_cond_Sd': _L1_cond_in['Sd']}

def reference(x, fside_BxSxS_0, itok_B_0_5, fside_Bx8_0, condB_sharedgateprob, L0_cond_braak_embed, L1_cond_Wg, L1_cond_Wu, L1_cond_Wd, L1_cond_Sg, L1_cond_Su, L1_cond_Sd):
    import jax
    import jax.numpy as jnp

    def _L0_cond_ref(query, key, value, braak_embed, braak_stages):
        import jax, jax.numpy as jnp
        import numpy as np
        B, S, D = (8, 256, 256)
        NUM_STAGES = 6
        bias = braak_embed[braak_stages][..., None]
        q = query + bias
        attn = jnp.einsum('bsd,btd->bst', q, key)
        attn = jax.nn.softmax(attn, axis=-1)
        return jnp.einsum('bst,btd->bsd', attn, value)

    def _L1_cond_ref(hidden_states, gating_probs, shared_gate_prob, Wg, Wu, Wd, Sg, Su, Sd):
        import jax, jax.numpy as jnp
        import numpy as np
        E, B, S, D, F = (8, 2, 256, 256, 1024)
        h = hidden_states
        g = jnp.einsum('bsd,edf->ebsf', h, Wg)
        u = jnp.einsum('bsd,edf->ebsf', h, Wu)
        expert_outs = jnp.einsum('ebsf,efd->ebsd', jax.nn.silu(g) * u, Wd)
        expert_output = jnp.einsum('be,ebsd->bsd', gating_probs, expert_outs)
        shared = jnp.einsum('bsf,fd->bsd', jax.nn.silu(h @ Sg) * (h @ Su), Sd)
        sg = shared_gate_prob[:, :, None]
        return (1.0 - sg) * expert_output + sg * shared
    x = x + _L0_cond_ref(x, fside_BxSxS_0, fside_BxSxS_0, L0_cond_braak_embed, itok_B_0_5)
    x = x + _L1_cond_ref(x, fside_Bx8_0, condB_sharedgateprob[:, None], L1_cond_Wg, L1_cond_Wu, L1_cond_Wd, L1_cond_Sg, L1_cond_Su, L1_cond_Sd)
    return x

_drawn_inputs = setup_inputs


def setup_inputs(seed=0):
    import zlib

    import numpy as np

    out = dict(_drawn_inputs(seed))
    spreads = {}
    factors = {}
    for name, (base, spread) in spreads.items():
        noise = np.random.default_rng([zlib.crc32(name.encode()), seed]).standard_normal(out[name].shape)
        drawn = base * np.exp(spread * noise) if base else spread * noise
        out[name] = jnp.asarray(drawn.astype(out[name].dtype))
    for name, factor in factors.items():
        out[name] = (out[name] * factor).astype(out[name].dtype)
    return out
```

```python
from contextlib import ExitStack

import concourse.bass as bass
from concourse import mybir

P = 128
F32 = mybir.dt.float32
F32R = mybir.dt.float32r
I32 = mybir.dt.int32
ALU = mybir.AluOpType
ACT = mybir.ActivationFunctionType
AX_X = mybir.AxisListType.X


def build(nc, x, key, stage, gating, shared_gate, embed, wg, wu, wd, sg, su, sd, out):
    B, S, D = x.shape
    E, _, F = wg.shape
    STAGES = embed.shape[0]
    DT = D // P
    ST = S // P
    FT = F // P
    BLK = 512
    BPB = BLK // S
    NB = B * S // BLK
    STEPS = NB * FT
    LAG = 2
    LAST = STEPS - FT
    assert D == 2 * P and S == 2 * P and NB == 4 and FT == 8 and B % 2 == 0

    with ExitStack() as ctx:
        def sb(name, shape, dt=F32):
            return ctx.enter_context(nc.sbuf_tensor(name, shape, dt))

        def sem(name):
            return ctx.enter_context(nc.semaphore(name))

        ident = sb("ident", [P, P])
        xn = [sb(f"xn{i}", [P, ST, D]) for i in range(2)]
        kn = [sb(f"kn{i}", [P, ST, D]) for i in range(2)]
        vn = [sb(f"vn{i}", [P, ST, D]) for i in range(2)]
        bias = sb("bias", [P, B, S])
        stage_sb = sb("stage_sb", [1, B], I32)
        qT = [sb(f"qT{i}", [P, DT, S]) for i in range(2)]
        kT = [sb(f"kT{i}", [P, DT, S]) for i in range(2)]
        probs = [sb(f"probs{i}", [P, ST, S]) for i in range(2)]
        probsT = sb("probsT", [P, ST, S])
        row_max = sb("row_max", [P, 2, ST])
        neg_max = sb("neg_max", [P, 2, ST])
        row_sum = sb("row_sum", [P, 2, ST])
        row_inv = sb("row_inv", [P, 2, ST])
        acc = sb("acc", [P, DT, B * S])
        x1hi = sb("x1hi", [P, DT, B * S], F32R)
        x1lo = sb("x1lo", [P, DT, B * S], F32R)
        gate_bc = sb("gate_bc", [P, B * E])
        shared_bc = sb("shared_bc", [P, B])
        unshared = sb("unshared", [P, B])
        coef = sb("coef", [P, (E + 1) * B])
        up_in = sb("up_in", [P, 2 * DT, F])
        down_in = sb("down_in", [P, FT, D])
        up_hi = sb("up_hi", [P, 2 * DT, F], F32R)
        up_lo = sb("up_lo", [P, 2 * DT, F], F32R)
        down_hi = sb("down_hi", [P, FT, D], F32R)
        down_lo = sb("down_lo", [P, FT, D], F32R)
        silu = [sb(f"silu{i}", [P, BLK]) for i in range(2)]
        h = [sb(f"h{i}", [P, BLK]) for i in range(2)]
        h_hi = [sb(f"h_hi{i}", [P, BLK], F32R) for i in range(2)]
        h_lo = [sb(f"h_lo{i}", [P, BLK], F32R) for i in range(2)]
        y = [sb(f"y{i}", [P, 2, D]) for i in range(2 * NB)]

        bank = [ctx.enter_context(nc.psum_tensor(f"bank{i}", [P, 512], F32)) for i in range(8)]
        xT_ps, g_ps = bank[0:2], bank[0:2]
        kT_ps, u_ps = bank[2:4], bank[2:4]
        s_ps, probsT_ps, attn_ps = bank[4:6], bank[6], bank[7]
        down_ps = [bank[4:6], bank[6:8]]

        ident_zeroed = sem("ident_zeroed")
        ident_ready = sem("ident_ready")
        stage_loaded = sem("stage_loaded")
        first_bias_loaded = [sem(f"first_bias_loaded{i}") for i in range(2)]
        bias_loaded = sem("bias_loaded")
        x_loaded = [sem(f"x_loaded{i}") for i in range(2)]
        k_loaded = [sem(f"k_loaded{i}") for i in range(2)]
        v_loaded = [sem(f"v_loaded{i}") for i in range(2)]
        gates_loaded = sem("gates_loaded")
        unshared_ready = sem("unshared_ready")
        coef_ready = sem("coef_ready")
        xT_done = sem("xT_done")
        kT_done = sem("kT_done")
        xT_copied = sem("xT_copied")
        kT_copied = sem("kT_copied")
        q_ready = sem("q_ready")
        scores_done = sem("scores_done")
        max_ready = sem("max_ready")
        neg_ready = sem("neg_ready")
        exp_done = sem("exp_done")
        inv_ready = sem("inv_ready")
        probs_ready = sem("probs_ready")
        probsT_done = sem("probsT_done")
        probsT_copied = sem("probsT_copied")
        attn_done = sem("attn_done")
        x1_ready = sem("x1_ready")
        x1hi_ready = sem("x1hi_ready")
        x1lo_ready = sem("x1lo_ready")
        w_loaded = sem("w_loaded")
        w_hi_ready = sem("w_hi_ready")
        w_ready = sem("w_ready")
        g_done = sem("g_done")
        u_done = sem("u_done")
        silu_done = sem("silu_done")
        h_done = sem("h_done")
        h_hi_ready = sem("h_hi_ready")
        h_ready = sem("h_ready")
        down_done = sem("down_done")
        down_free = sem("down_free")
        out_T_done = sem("out_T_done")
        y_ready = sem("y_ready")
        y_stored = sem("y_stored")

        UP_LOADS = 3 * 16

        def cols(b, n=1):
            return bass.ds(b * S, n * S)

        def w_tile(up, down, f):
            return up[:, :, f * P:(f + 1) * P], down[:, f, :]

        block = ctx.enter_context(nc.Block())

        @block.sync
        def _(sp):
            def load_rows(dst, src, b, loaded):
                sp.dma_start(dst, src[bass.ds(b, 1)].rearrange("o (t p) d -> p (o t) d", p=P)).then_inc(loaded, 16)

            sp.dma_start(stage_sb[:, :], stage.rearrange("(o b) -> o b", o=1)).then_inc(stage_loaded, 16)
            for b in range(2):
                load_rows(xn[b][:, :, :], x, b, x_loaded[b])
                load_rows(kn[b][:, :, :], key, b, k_loaded[b])
            sp.wait_ge(stage_loaded, 16)
            for b in range(B):
                row = sp.value_load(stage_sb[0:1, b:b + 1], min_val=0, max_val=STAGES - 1)
                sp.dma_start(bias[:, b, :], embed[bass.ds(row, 1), :].partition_broadcast(P)).then_inc(
                    first_bias_loaded[b] if b < 2 else bias_loaded, 16)
                if b < 2:
                    load_rows(vn[b][:, :, :], key, b, v_loaded[b])
            sp.dma_start(gate_bc[:, :], gating.rearrange("(o b) e -> o (b e)", o=1).partition_broadcast(P)).then_inc(gates_loaded, 16)
            sp.dma_start(shared_bc[:, :], shared_gate.rearrange("(o b) -> o b", o=1).partition_broadcast(P)).then_inc(gates_loaded, 16)

            def load_xk(b, slot):
                sp.wait_ge(xT_done, b - 1)
                load_rows(xn[slot][:, :, :], x, b, x_loaded[slot])
                sp.wait_ge(kT_done, b - 1)
                load_rows(kn[slot][:, :, :], key, b, k_loaded[slot])

            def load_v(b, slot):
                sp.wait_ge(attn_done, b - 1)
                load_rows(vn[slot][:, :, :], key, b, v_loaded[slot])

            load_xk(2, 0)
            with sp.Fori(2, B - 3, 2) as b:
                for i in range(2):
                    load_v(b + i, i)
                    load_xk(b + i + 1, (i + 1) % 2)
            load_v(B - 2, 0)
            load_xk(B - 1, 1)
            load_v(B - 1, 1)

            def load_expert(g_src, u_src, d_src, e):
                sp.wait_ge(w_ready, e * FT)
                sp.dma_start(up_in[:, 0:DT, :], g_src).then_inc(w_loaded, 16)
                sp.dma_start(up_in[:, DT:2 * DT, :], u_src).then_inc(w_loaded, 16)
                sp.dma_start(down_in[:, :, :], d_src).then_inc(w_loaded, 16)

            with sp.Fori(1, E) as e:
                load_expert(wg[bass.ds(e, 1)].rearrange("o (t p) f -> p (o t) f", p=P),
                            wu[bass.ds(e, 1)].rearrange("o (t p) f -> p (o t) f", p=P),
                            wd[bass.ds(e, 1)].rearrange("o (t p) d -> p (o t) d", p=P), e)
            load_expert(sg.rearrange("(t p) f -> p t f", p=P), su.rearrange("(t p) f -> p t f", p=P),
                        sd.rearrange("(t p) d -> p t d", p=P), E)

            rows = out.rearrange("b s d -> (b s) d").rearrange("(n t p) d -> n p t d", t=2, p=P)
            for n in range(2 * NB):
                sp.wait_ge(y_ready, n + 1)
                sp.dma_start(rows[n], y[n][:, :, :]).then_inc(y_stored, 16)
            sp.wait_ge(y_stored, 2 * NB * 16)

        @block.tensor
        def _(pe):
            def transpose_xk(b, slot):
                pe.wait_ge(x_loaded[slot], 16 * (b // 2) + 16)
                for d in range(DT):
                    for t in range(ST):
                        last = pe.transpose(xT_ps[slot][:, d * S + t * P:d * S + (t + 1) * P],
                                            xn[slot][:, t, d * P:(d + 1) * P], ident[:, :])
                last.then_inc(xT_done, 1)
                pe.wait_ge(k_loaded[slot], 16 * (b // 2) + 16)
                for d in range(DT):
                    for t in range(ST):
                        last = pe.transpose(kT_ps[slot][:, d * S + t * P:d * S + (t + 1) * P],
                                            kn[slot][:, t, d * P:(d + 1) * P], ident[:, :])
                last.then_inc(kT_done, 1)

            def scores(b, slot):
                pe.wait_ge(q_ready, b + 1)
                pe.wait_ge(kT_copied, b + 1)
                for t in range(ST):
                    for d in range(DT):
                        last = pe.matmul(s_ps[slot][:, t * S:(t + 1) * S], qT[slot][:, d, t * P:(t + 1) * P],
                                         kT[slot][:, d, :], start=(d == 0), stop=(d == DT - 1))
                last.then_inc(scores_done, 1)

            def transpose_probs(b, slot):
                pe.wait_ge(probs_ready, b + 1)
                for k in range(ST):
                    for t in range(ST):
                        last = pe.transpose(probsT_ps[:, k * S + t * P:k * S + (t + 1) * P],
                                            probs[slot][:, t, k * P:(k + 1) * P], ident[:, :])
                last.then_inc(probsT_done, 1)

            def attend(b, slot):
                pe.wait_ge(v_loaded[slot], 16 * (b // 2) + 16)
                pe.wait_ge(probsT_copied, b + 1)
                for d in range(DT):
                    for k in range(ST):
                        last = pe.matmul(attn_ps[:, d * S:(d + 1) * S], vn[slot][:, k, d * P:(d + 1) * P],
                                         probsT[:, k, :], start=(k == 0), stop=(k == ST - 1))
                last.then_inc(attn_done, 1)

            def up(j):
                n, f = j // FT % NB, j % FT
                for ps, at, done in ((g_ps, 0, g_done), (u_ps, DT, u_done)):
                    k = 0
                    for w, a in ((up_hi, x1lo), (up_hi, x1hi), (up_lo, x1hi)):
                        for d in range(DT):
                            last = pe.matmul(ps[j % 2][:, :], w[:, at + d, f * P:(f + 1) * P],
                                             a[:, d, n * BLK:(n + 1) * BLK], start=(k == 0), stop=(k == 3 * DT - 1))
                            k += 1
                    last.then_inc(done, 1)

            def down(j):
                n, f = j // FT % NB, j % FT
                for d in range(DT):
                    for k, (w, a) in enumerate(((down_hi, h_lo), (down_hi, h_hi), (down_lo, h_hi))):
                        last = pe.matmul(down_ps[n % 2][d][:, :], w[:, f, d * P:(d + 1) * P], a[j % 2][:, :],
                                         start=(f == 0 and k == 0), stop=(f == FT - 1 and k == 2))
                last.then_inc(down_done, 1)

            def expert_steps(e, last):
                for j in range(STEPS):
                    a = j + LAG
                    if a < STEPS or not last:
                        pe.wait_ge(h_done, e * STEPS + a - 1)
                        if a < FT:
                            pe.wait_ge(w_ready, e * FT + a + 1)
                        if a >= STEPS:
                            pe.wait_ge(w_ready, e * FT + FT + a - STEPS + 1)
                        if a % FT == 0:
                            pe.wait_ge(x1lo_ready, BPB * (a // FT % NB + 1))
                        up(a)
                    pe.wait_ge(h_ready, e * STEPS + j + 1)
                    if j % FT == 0:
                        pe.wait_ge(down_free, e * NB + j // FT + 1)
                        if last and j // FT >= 2:
                            pe.wait_ge(y_ready, 2 * (j // FT - 1))
                    down(j)
                    if last and j >= FT and j % FT == LAG:
                        transpose_out(j // FT - 1)
                if last:
                    transpose_out(NB - 1)

            def transpose_out(n):
                pe.wait_ge(down_free, E * NB + n + 3)
                for half in range(2):
                    for t in range(2):
                        for d in range(DT):
                            c = n * BLK + (2 * half + t) * P
                            last = pe.transpose(down_ps[n % 2][half][:, t * D + d * P:t * D + (d + 1) * P],
                                                acc[:, d, c:c + P], ident[:, :])
                    last.then_inc(out_T_done, 1)

            pe.wait_ge(ident_ready, 1)
            transpose_xk(0, 0)
            scores(0, 0)
            transpose_xk(1, 1)
            with pe.Fori(1, B - 2, 2) as b:
                for i in range(2):
                    slot = (1 + i) % 2
                    transpose_probs(b + (i - 1), 1 - slot)
                    scores(b + i, slot)
                    attend(b + (i - 1), 1 - slot)
                    transpose_xk(b + (i + 1), 1 - slot)
            transpose_probs(B - 2, 0)
            scores(B - 1, 1)
            attend(B - 2, 0)
            pe.wait_ge(w_ready, 1)
            pe.wait_ge(x1lo_ready, BPB)
            up(0)
            transpose_probs(B - 1, 1)
            pe.wait_ge(w_ready, 2)
            up(1)
            attend(B - 1, 1)

            with pe.Fori(0, E) as e:
                expert_steps(e, False)
            expert_steps(E, True)

        @block.scalar
        def _(act):
            act.dma_start(up_in[:, 0:DT, :], wg[0].rearrange("(t p) f -> p t f", p=P)).then_inc(w_loaded, 16)
            act.dma_start(up_in[:, DT:2 * DT, :], wu[0].rearrange("(t p) f -> p t f", p=P)).then_inc(w_loaded, 16)
            act.dma_start(down_in[:, :, :], wd[0].rearrange("(t p) d -> p t d", p=P)).then_inc(w_loaded, 16)

            def copy_xk(b, slot):
                act.wait_ge(xT_done, b + 1)
                act.copy(acc[:, :, cols(b)], xT_ps[slot][:, :].rearrange("p (d s) -> p d s", d=DT)).then_inc(xT_copied, 1)
                act.wait_ge(kT_done, b + 1)
                act.copy(kT[slot][:, :, :], kT_ps[slot][:, :].rearrange("p (d s) -> p d s", d=DT)).then_inc(kT_copied, 1)

            def exponentials(b, slot):
                act.wait_ge(neg_ready, b + 1)
                for t in range(ST):
                    last = act.activation(probs[slot][:, t, :], s_ps[slot][:, t * S:(t + 1) * S], ACT.Exp,
                                          bias=neg_max[:, slot, t:t + 1], accum_out=row_sum[:, slot, t:t + 1])
                last.then_inc(exp_done, 1)

            def copy_probsT(b):
                act.wait_ge(probsT_done, b + 1)
                act.copy(probsT[:, :, :], probsT_ps[:, :].rearrange("p (k s) -> p k s", k=ST)).then_inc(probsT_copied, 1)

            def x1_high(b):
                act.wait_ge(x1_ready, b + 1)
                act.copy(x1hi[:, :, cols(b)], acc[:, :, cols(b)]).then_inc(x1hi_ready, 1)

            def gate(t, j):
                act.wait_ge(g_done, t + 1)
                act.activation(silu[j % 2][:, :], g_ps[j % 2][:, :], ACT.Silu).then_inc(silu_done, 1)

            def weights_high(e, f):
                act.wait_ge(w_loaded, (e + 2) * UP_LOADS)
                act.wait_ge(down_done, e * STEPS + LAST + f + 1)
                (up_s, down_s), (up_d, down_d) = w_tile(up_in, down_in, f), w_tile(up_hi, down_hi, f)
                act.copy(up_d, up_s)
                act.copy(down_d, down_s).then_inc(w_hi_ready, 1)

            copy_xk(0, 0)
            exponentials(0, 0)
            copy_xk(1, 1)
            with act.Fori(1, B - 2, 2) as b:
                for i in range(2):
                    slot = (1 + i) % 2
                    copy_probsT(b + (i - 1))
                    exponentials(b + i, slot)
                    copy_xk(b + (i + 1), 1 - slot)
                    x1_high(b + (i - 1))
            copy_probsT(B - 2)
            exponentials(B - 1, 1)
            x1_high(B - 2)
            copy_probsT(B - 1)
            gate(0, 0)
            gate(1, 1)
            x1_high(B - 1)

            with act.Fori(0, E) as e:
                for j in range(STEPS):
                    gate(e * STEPS + j + LAG, j + LAG)
                    if j >= LAST:
                        weights_high(e, j - LAST)
            for j in range(STEPS):
                if j + LAG < STEPS:
                    gate(E * STEPS + j + LAG, j + LAG)
                if j > FT and j % FT == LAG:
                    n = j // FT - 1
                    for half in range(2):
                        act.wait_ge(out_T_done, 2 * n + half + 1)
                        act.copy(y[2 * n + half][:, :, :],
                                 down_ps[n % 2][half][:, :].rearrange("p (t d) -> p t d", t=2)).then_inc(y_ready, 1)
            for half in range(2):
                act.wait_ge(out_T_done, 2 * NB - 1 + half)
                act.copy(y[2 * NB - 2 + half][:, :, :],
                         down_ps[(NB - 1) % 2][half][:, :].rearrange("p (t d) -> p t d", t=2)).then_inc(y_ready, 1)

        @block.vector
        def _(dve):
            def queries(b, slot):
                dve.wait_ge(xT_copied, b + 1)
                if isinstance(b, int):
                    dve.wait_ge(first_bias_loaded[b], 16)
                else:
                    dve.wait_ge(bias_loaded, 16 * (B - 2))
                dve.tensor_tensor(qT[slot][:, :, :], acc[:, :, cols(b)],
                                  bias[:, bass.ds(b, 1), :].broadcast_to([P, DT, S]), ALU.add).then_inc(q_ready, 1)

            def maxima(b, slot):
                dve.wait_ge(scores_done, b + 1)
                dve.tensor_reduce(row_max[:, slot, :], s_ps[slot][:, :].rearrange("p (t s) -> p t s", t=ST),
                                  AX_X, ALU.max).then_inc(max_ready, 1)
                dve.wait_ge(max_ready, b + 1)
                dve.tensor_scalar(neg_max[:, slot, :], row_max[:, slot, :], -1.0, None, ALU.mult).then_inc(neg_ready, 1)

            def normalise(b, slot):
                dve.wait_ge(exp_done, b + 1)
                dve.reciprocal(row_inv[:, slot, :], row_sum[:, slot, :]).then_inc(inv_ready, 1)
                dve.wait_ge(inv_ready, b + 1)
                for t in range(ST):
                    last = dve.tensor_scalar(probs[slot][:, t, :], probs[slot][:, t, :],
                                             row_inv[:, slot, t:t + 1], None, ALU.mult)
                last.then_inc(probs_ready, 1)

            def residual(b):
                dve.wait_ge(attn_done, b + 1)
                return dve.tensor_tensor(acc[:, :, cols(b)], attn_ps[:, :].rearrange("p (d s) -> p d s", d=DT),
                                         acc[:, :, cols(b)], ALU.add).then_inc(x1_ready, 1)

            def hidden(t, j):
                dve.wait_ge(silu_done, t + 1)
                dve.wait_ge(u_done, t + 1)
                dve.tensor_tensor(h[j % 2][:, :], u_ps[j % 2][:, :], silu[j % 2][:, :], ALU.mult).then_inc(h_done, 1)
                dve.wait_ge(h_done, t + 1)
                if j >= LAG:
                    dve.wait_ge(down_done, t - 1)
                dve.tensor_copy(h_hi[j % 2][:, :], h[j % 2][:, :]).then_inc(h_hi_ready, 1)
                dve.wait_ge(h_hi_ready, t + 1)
                dve.tensor_tensor(h_lo[j % 2][:, :], h[j % 2][:, :], h_hi[j % 2][:, :].bitcast(F32),
                                  ALU.subtract).then_inc(h_ready, 1)

            def take_block(e, n):
                dve.wait_ge(down_done, e * STEPS + (n + 1) * FT)
                for i in range(BPB):
                    b = BPB * n + i
                    for d in range(DT):
                        last = dve.scalar_tensor_tensor(acc[:, d, b * S:(b + 1) * S], down_ps[n % 2][d][:, i * S:(i + 1) * S],
                                                        coef[:, bass.ds(e * B + b, 1)], acc[:, d, b * S:(b + 1) * S],
                                                        ALU.mult, ALU.add)
                last.then_inc(down_free, 1)

            def weights_low(e, f):
                dve.wait_ge(w_hi_ready, (e + 1) * FT + f + 1)
                up_s, down_s = w_tile(up_in, down_in, f)
                up_h, down_h = w_tile(up_hi, down_hi, f)
                up_l, down_l = w_tile(up_lo, down_lo, f)
                dve.tensor_tensor(up_l, up_s, up_h.bitcast(F32), ALU.subtract)
                dve.tensor_tensor(down_l, down_s, down_h.bitcast(F32), ALU.subtract).then_inc(w_ready, 1)

            queries(0, 0)
            maxima(0, 0)
            normalise(0, 0)
            queries(1, 1)
            with dve.Fori(1, B - 2, 2) as b:
                for i in range(2):
                    slot = (1 + i) % 2
                    maxima(b + i, slot)
                    normalise(b + i, slot)
                    residual(b + (i - 1))
                    queries(b + (i + 1), 1 - slot)
            maxima(B - 1, 1)
            normalise(B - 1, 1)
            residual(B - 2)
            hidden(0, 0)
            residual(B - 1)
            dve.wait_ge(x1_ready, B)
            dve.tensor_copy(row_max[:, 0, :], row_max[:, 1, :]).then_inc(down_free, 2)
            hidden(1, 1)
            dve.wait_ge(coef_ready, 2)

            with dve.Fori(0, E) as e:
                for j in range(STEPS):
                    hidden(e * STEPS + j + LAG, j + LAG)
                    if j >= LAST:
                        weights_low(e, j - LAST)
                    if j % FT == FT - 1:
                        take_block(e, j // FT)
            for j in range(STEPS):
                if j + LAG < STEPS:
                    hidden(E * STEPS + j + LAG, j + LAG)
                if j % FT == FT - 1:
                    take_block(E, j // FT)

        @block.gpsimd
        def _(pool):
            pool.memset(ident[:, :], 0.0).then_inc(ident_zeroed, 1)
            pool.wait_ge(ident_zeroed, 1)
            pool.affine_select(out=ident[:, :], in_=ident[:, :], compare_op=ALU.not_equal, fill=1.0, base=0,
                               pattern=[[-1, P]], channel_multiplier=1).then_inc(ident_ready, 1)

            pool.wait_ge(gates_loaded, 32)
            pool.tensor_scalar(unshared[:, :], shared_bc[:, :], -1.0, 1.0, ALU.mult, ALU.add).then_inc(unshared_ready, 1)
            pool.tensor_copy(coef[:, E * B:(E + 1) * B], shared_bc[:, :]).then_inc(coef_ready, 1)
            pool.wait_ge(unshared_ready, 1)
            pool.tensor_tensor(coef[:, 0:E * B].rearrange("p (e b) -> p e b", e=E),
                               gate_bc[:, :].rearrange("p (b e) -> p e b", b=B),
                               unshared[:, :].rearrange("p (o b) -> p o b", o=1).broadcast_to([P, E, B]),
                               ALU.mult).then_inc(coef_ready, 1)

            def x1_low(b):
                pool.wait_ge(x1hi_ready, b + 1)
                pool.tensor_tensor(x1lo[:, :, cols(b)], acc[:, :, cols(b)], x1hi[:, :, cols(b)].bitcast(F32),
                                   ALU.subtract).then_inc(x1lo_ready, 1)

            def split_first(f):
                up_s, down_s = w_tile(up_in, down_in, f)
                up_h, down_h = w_tile(up_hi, down_hi, f)
                up_l, down_l = w_tile(up_lo, down_lo, f)
                pool.tensor_copy(up_h, up_s)
                pool.tensor_copy(down_h, down_s).then_inc(w_hi_ready, 1)
                pool.wait_ge(w_hi_ready, f + 1)
                pool.tensor_tensor(up_l, up_s, up_h.bitcast(F32), ALU.subtract)
                pool.tensor_tensor(down_l, down_s, down_h.bitcast(F32), ALU.subtract).then_inc(w_ready, 1)

            pool.wait_ge(w_loaded, UP_LOADS)
            for f in range(FT):
                split_first(f)
                x1_low(f)


_INS = ["x", "fside_BxSxS_0", "itok_B_0_5", "fside_Bx8_0", "condB_sharedgateprob", "L0_cond_braak_embed",
        "L1_cond_Wg", "L1_cond_Wu", "L1_cond_Wd", "L1_cond_Sg", "L1_cond_Su", "L1_cond_Sd"]


def kernel(**inputs):
    import numpy as np
    import concourse.bacc as bacc
    from concourse.bass_utils import run_bass_kernel_spmd

    nc = bacc.Bacc("TRN2", target_bir_lowering=False, num_devices=1)
    arrays, args = {}, []
    for name in _INS:
        a = np.ascontiguousarray(inputs[name])
        arrays[f"in_{name}"] = a
        args.append(nc.dram_tensor(f"in_{name}", a.shape, mybir.dt.from_np(a.dtype), kind="ExternalInput").ap())
    out = nc.dram_tensor("out", inputs["x"].shape, F32, kind="ExternalOutput").ap()
    build(nc, *args, out)
    r = run_bass_kernel_spmd(nc, [arrays], core_ids=[0])
    return r.results[0]["out"]
```

```python
from contextlib import ExitStack

import concourse.bass as bass
from concourse import mybir

P = 128
F32 = mybir.dt.float32
F32R = mybir.dt.float32r
I32 = mybir.dt.int32
ALU = mybir.AluOpType
ACT = mybir.ActivationFunctionType
AX_X = mybir.AxisListType.X


def build(nc, x, key, stage, gating, shared_gate, embed, wg, wu, wd, sg, su, sd, out):
    B, S, D = x.shape
    E, _, F = wg.shape
    STAGES = embed.shape[0]
    DT = D // P
    ST = S // P
    FT = F // P
    BLK = 512
    BPB = BLK // S
    NB = B * S // BLK
    STEPS = NB * FT
    LAG = 2
    LAST = STEPS - FT
    assert D == 2 * P and S == 2 * P and NB == 4 and FT == 8 and B % 2 == 0

    with ExitStack() as ctx:
        def sb(name, shape, dt=F32):
            return ctx.enter_context(nc.sbuf_tensor(name, shape, dt))

        def sem(name):
            return ctx.enter_context(nc.semaphore(name))

        ident = sb("ident", [P, P])
        xn = [sb(f"xn{i}", [P, ST, D]) for i in range(2)]
        kn = [sb(f"kn{i}", [P, ST, D]) for i in range(2)]
        vn = [sb(f"vn{i}", [P, ST, D]) for i in range(2)]
        bias = sb("bias", [P, B, S])
        table_probe = sb("table_probe", [P, 1])
        stage_sb = sb("stage_sb", [1, B], I32)
        qT = [sb(f"qT{i}", [P, DT, S]) for i in range(2)]
        kT = [sb(f"kT{i}", [P, DT, S]) for i in range(2)]
        probs = [sb(f"probs{i}", [P, ST, S]) for i in range(2)]
        probsT = sb("probsT", [P, ST, S])
        neg_max = sb("neg_max", [P, 2, ST])
        row_sum = sb("row_sum", [P, 2, ST])
        row_inv = sb("row_inv", [P, 2, ST])
        acc = sb("acc", [P, DT, B * S])
        x1hi = sb("x1hi", [P, DT, B * S], F32R)
        x1lo = sb("x1lo", [P, DT, B * S], F32R)
        gate_bc = sb("gate_bc", [P, B * E])
        shared_bc = sb("shared_bc", [P, B])
        unshared = sb("unshared", [P, B])
        coef = sb("coef", [P, (E + 1) * B])
        up_in = sb("up_in", [P, 2 * DT, F])
        down_in = sb("down_in", [P, FT, D])
        up_hi = sb("up_hi", [P, 2 * DT, F], F32R)
        up_lo = sb("up_lo", [P, 2 * DT, F], F32R)
        down_hi = sb("down_hi", [P, FT, D], F32R)
        down_lo = sb("down_lo", [P, FT, D], F32R)
        silu = [sb(f"silu{i}", [P, BLK]) for i in range(2)]
        h = [sb(f"h{i}", [P, BLK]) for i in range(2)]
        h_hi = [sb(f"h_hi{i}", [P, BLK], F32R) for i in range(2)]
        h_lo = [sb(f"h_lo{i}", [P, BLK], F32R) for i in range(2)]
        y = [sb(f"y{i}", [P, 2, D]) for i in range(2 * NB)]

        bank = [ctx.enter_context(nc.psum_tensor(f"bank{i}", [P, 512], F32)) for i in range(8)]
        xT_ps, g_ps = bank[0:2], bank[0:2]
        kT_ps, u_ps = bank[2:4], bank[2:4]
        s_ps, probsT_ps, attn_ps = bank[4:6], bank[6], bank[7]
        down_ps = [bank[4:6], bank[6:8]]

        out_ps = [down_ps[n % 2] for n in range(NB - 1)] + [g_ps]

        ident_zeroed = sem("ident_zeroed")
        ident_ready = sem("ident_ready")
        stage_loaded = sem("stage_loaded")
        first_bias_loaded = [sem(f"first_bias_loaded{i}") for i in range(2)]
        bias_loaded = sem("bias_loaded")
        x_loaded = [sem(f"x_loaded{i}") for i in range(2)]
        k_loaded = [sem(f"k_loaded{i}") for i in range(2)]
        v_loaded = [sem(f"v_loaded{i}") for i in range(2)]
        gates_loaded = sem("gates_loaded")
        unshared_ready = sem("unshared_ready")
        coef_ready = sem("coef_ready")
        xT_done = sem("xT_done")
        kT_done = sem("kT_done")
        xT_copied = sem("xT_copied")
        kT_copied = sem("kT_copied")
        q_ready = sem("q_ready")
        scores_done = sem("scores_done")
        max_ready = sem("max_ready")
        exp_done = sem("exp_done")
        inv_ready = sem("inv_ready")
        probs_ready = sem("probs_ready")
        probsT_done = sem("probsT_done")
        probsT_copied = sem("probsT_copied")
        attn_done = sem("attn_done")
        x1_ready = sem("x1_ready")
        x1hi_ready = sem("x1hi_ready")
        x1lo_ready = sem("x1lo_ready")
        first_w_loaded = sem("first_w_loaded")
        w_loaded = sem("w_loaded")
        w_hi_ready = sem("w_hi_ready")
        w_ready = sem("w_ready")
        g_done = sem("g_done")
        u_done = sem("u_done")
        silu_done = sem("silu_done")
        h_done = sem("h_done")
        h_hi_ready = sem("h_hi_ready")
        h_ready = sem("h_ready")
        down_done = sem("down_done")
        down_free = sem("down_free")
        out_T_done = sem("out_T_done")
        y_ready = sem("y_ready")
        y_stored = sem("y_stored")

        W_LOADS = 3 * 16

        def cols(b, n=1):
            return bass.ds(b * S, n * S)

        def w_tile(up, down, f):
            return up[:, :, bass.ds(f * P, P)], down[:, bass.ds(f, 1), :]

        block = ctx.enter_context(nc.Block())

        def load_bias(eng, b):
            row = eng.value_load(stage_sb[0:1, b:b + 1], min_val=0, max_val=STAGES - 1)
            return eng.dma_start(bias[:, b, :], embed[bass.ds(row, 1), :].partition_broadcast(P))

        @block.sync
        def _(sp):
            def load_rows(dst, src, b, loaded):
                sp.dma_start(dst, src[bass.ds(b, 1)].rearrange("o (t p) d -> p (o t) d", p=P)).then_inc(loaded, 16)

            load_rows(xn[0][:, :, :], x, 0, x_loaded[0])
            load_rows(kn[0][:, :, :], key, 0, k_loaded[0])
            load_rows(xn[1][:, :, :], x, 1, x_loaded[1])
            load_rows(kn[1][:, :, :], key, 1, k_loaded[1])
            sp.wait_ge(stage_loaded, 16)
            for b in range(2):
                load_bias(sp, b).then_inc(first_bias_loaded[b], 16)
            for b in range(2):
                load_rows(vn[b][:, :, :], key, b, v_loaded[b])

            def load_xk(b, slot):
                sp.wait_ge(xT_done, b - 1)
                load_rows(xn[slot][:, :, :], x, b, x_loaded[slot])
                sp.wait_ge(kT_done, b - 1)
                load_rows(kn[slot][:, :, :], key, b, k_loaded[slot])

            def load_v(b, slot):
                sp.wait_ge(attn_done, b - 1)
                load_rows(vn[slot][:, :, :], key, b, v_loaded[slot])

            def load_expert(g_src, u_src, d_src):
                sp.dma_start(up_in[:, 0:DT, :], g_src).then_inc(w_loaded, 16)
                sp.dma_start(up_in[:, DT:2 * DT, :], u_src).then_inc(w_loaded, 16)
                sp.dma_start(down_in[:, :, :], d_src).then_inc(w_loaded, 16)

            load_xk(2, 0)
            load_xk(3, 1)
            for b in range(2, B):
                load_v(b, b % 2)
                if b + 2 < B:
                    load_xk(b + 2, b % 2)
                if b - 2 < FT // 2:
                    c = b - 2
                    if c:
                        sp.wait_ge(first_w_loaded, c * W_LOADS)
                    cut = slice(2 * c * P, 2 * (c + 1) * P)
                    for at, w in ((0, wg), (DT, wu)):
                        sp.dma_start(up_in[:, at:at + DT, cut],
                                     w[0].rearrange("(t p) f -> p t f", p=P)[:, :, cut]).then_inc(first_w_loaded, 16)
                    sp.dma_start(down_in[:, 2 * c:2 * c + 2, :],
                                 wd[0].rearrange("(t p) d -> p t d", p=P)[:, 2 * c:2 * c + 2, :]).then_inc(first_w_loaded, 16)

            with sp.Fori(1, E) as e:
                sp.wait_ge(w_ready, e * FT)
                load_expert(wg[bass.ds(e, 1)].rearrange("o (t p) f -> p (o t) f", p=P),
                            wu[bass.ds(e, 1)].rearrange("o (t p) f -> p (o t) f", p=P),
                            wd[bass.ds(e, 1)].rearrange("o (t p) d -> p (o t) d", p=P))
            sp.wait_ge(w_ready, E * FT)
            load_expert(sg.rearrange("(t p) f -> p t f", p=P), su.rearrange("(t p) f -> p t f", p=P),
                        sd.rearrange("(t p) d -> p t d", p=P))

            rows = out.rearrange("b s d -> (b s) d").rearrange("(n t p) d -> n p t d", t=2, p=P)
            for n in range(2 * NB):
                sp.wait_ge(y_ready, n + 1)
                sp.dma_start(rows[n], y[n][:, :, :]).then_inc(y_stored, 16)
            sp.wait_ge(y_stored, 2 * NB * 16)

        @block.tensor
        def _(pe):
            def transpose_xk(b, slot):
                pe.wait_ge(x_loaded[slot], 16 * (b // 2) + 16)
                for d in range(DT):
                    for t in range(ST):
                        last = pe.transpose(xT_ps[slot][:, d * S + t * P:d * S + (t + 1) * P],
                                            xn[slot][:, t, d * P:(d + 1) * P], ident[:, :])
                last.then_inc(xT_done, 1)
                pe.wait_ge(k_loaded[slot], 16 * (b // 2) + 16)
                for d in range(DT):
                    for t in range(ST):
                        last = pe.transpose(kT_ps[slot][:, d * S + t * P:d * S + (t + 1) * P],
                                            kn[slot][:, t, d * P:(d + 1) * P], ident[:, :])
                last.then_inc(kT_done, 1)

            def scores(b, slot):
                pe.wait_ge(q_ready, b + 1)
                pe.wait_ge(kT_copied, b + 1)
                for t in range(ST):
                    for d in range(DT):
                        last = pe.matmul(s_ps[slot][:, t * S:(t + 1) * S], qT[slot][:, d, t * P:(t + 1) * P],
                                         kT[slot][:, d, :], start=(d == 0), stop=(d == DT - 1))
                last.then_inc(scores_done, 1)

            def transpose_probs(b, slot):
                pe.wait_ge(probs_ready, b + 1)
                for k in range(ST):
                    for t in range(ST):
                        last = pe.transpose(probsT_ps[:, k * S + t * P:k * S + (t + 1) * P],
                                            probs[slot][:, t, k * P:(k + 1) * P], ident[:, :])
                last.then_inc(probsT_done, 1)

            def attend(b, slot):
                pe.wait_ge(v_loaded[slot], 16 * (b // 2) + 16)
                pe.wait_ge(probsT_copied, b + 1)
                if not (isinstance(b, int) and b == 0):
                    pe.wait_ge(x1_ready, b)
                for d in range(DT):
                    for k in range(ST):
                        last = pe.matmul(attn_ps[:, d * S:(d + 1) * S], vn[slot][:, k, d * P:(d + 1) * P],
                                         probsT[:, k, :], start=(k == 0), stop=(k == ST - 1))
                last.then_inc(attn_done, 1)

            def up(j):
                n, f = j // FT % NB, j % FT
                for ps, at, done in ((g_ps, 0, g_done), (u_ps, DT, u_done)):
                    for d in range(DT):
                        for k, (w, a) in enumerate(((up_hi, x1lo), (up_hi, x1hi), (up_lo, x1hi))):
                            last = pe.matmul(ps[j % 2][:, :], w[:, at + d, f * P:(f + 1) * P],
                                             a[:, d, n * BLK:(n + 1) * BLK],
                                             start=(d == 0 and k == 0), stop=(d == DT - 1 and k == 2))
                    last.then_inc(done, 1)

            def down(j):
                n, f = j // FT % NB, j % FT
                for d in range(DT):
                    for k, (w, a) in enumerate(((down_hi, h_lo), (down_hi, h_hi), (down_lo, h_hi))):
                        last = pe.matmul(down_ps[n % 2][d][:, :], w[:, f, d * P:(d + 1) * P], a[j % 2][:, :],
                                         start=(f == 0 and k == 0), stop=(f == FT - 1 and k == 2))
                last.then_inc(down_done, 1)

            def expert_steps(e, last):
                for j in range(STEPS):
                    a = j + LAG
                    if a < STEPS or not last:
                        pe.wait_ge(h_done, e * STEPS + a - 1)
                        if a < FT:
                            pe.wait_ge(w_ready, e * FT + a + 1)
                        if a >= STEPS:
                            pe.wait_ge(w_ready, e * FT + FT + a - STEPS + 1)
                        if a % FT == 0:
                            pe.wait_ge(x1lo_ready, BPB * (a // FT % NB + 1))
                        up(a)
                    pe.wait_ge(h_ready, e * STEPS + j + 1)
                    if j % FT == 0:
                        pe.wait_ge(down_free, e * B + BPB * (j // FT + 1))
                        if last and j // FT >= 2:
                            pe.wait_ge(y_ready, 2 * (j // FT - 1))
                    down(j)
                    if last and j >= FT and j % FT == LAG:
                        transpose_out(j // FT - 1)
                if last:
                    transpose_out(NB - 1)

            def transpose_out(n):
                for half in range(2):
                    pe.wait_ge(down_free, E * B + BPB * (n + 2) + half + 1)
                    for t in range(2):
                        for d in range(DT):
                            c = n * BLK + (2 * half + t) * P
                            last = pe.transpose(out_ps[n][half][:, t * D + d * P:t * D + (d + 1) * P],
                                                acc[:, d, c:c + P], ident[:, :])
                    last.then_inc(out_T_done, 1)

            pe.wait_ge(ident_ready, 1)
            transpose_xk(0, 0)
            transpose_xk(1, 1)
            scores(0, 0)
            with pe.Fori(1, B - 2, 2) as b:
                for i in range(2):
                    slot = (1 + i) % 2
                    scores(b + i, slot)
                    transpose_probs(b + (i - 1), 1 - slot)
                    transpose_xk(b + (i + 1), 1 - slot)
                    attend(b + (i - 1), 1 - slot)
            scores(B - 1, 1)
            transpose_probs(B - 2, 0)
            pe.wait_ge(w_ready, 1)
            pe.wait_ge(x1lo_ready, BPB)
            up(0)
            attend(B - 2, 0)
            transpose_probs(B - 1, 1)
            pe.wait_ge(w_ready, 2)
            up(1)
            attend(B - 1, 1)

            with pe.Fori(0, E) as e:
                expert_steps(e, False)
            expert_steps(E, True)

        @block.scalar
        def _(act):
            act.dma_start(stage_sb[:, :], stage.rearrange("(o b) -> o b", o=1)).then_inc(stage_loaded, 16)
            act.wait_ge(ident_ready, 1)
            act.activation(table_probe[:, :], ident[:, 0:1], ACT.Exp)

            def copy_x(b, slot):
                act.wait_ge(xT_done, b + 1)
                act.copy(acc[:, :, cols(b)], xT_ps[slot][:, :].rearrange("p (d s) -> p d s", d=DT)).then_inc(xT_copied, 1)

            def copy_k(b, slot):
                act.wait_ge(kT_done, b + 1)
                act.copy(kT[slot][:, :, :], kT_ps[slot][:, :].rearrange("p (d s) -> p d s", d=DT)).then_inc(kT_copied, 1)

            def exponentials(b, slot):
                act.wait_ge(max_ready, b + 1)
                for t in range(ST):
                    act.activation(probs[slot][:, t, :], s_ps[slot][:, t * S:(t + 1) * S], ACT.Exp,
                                   bias=neg_max[:, slot, t:t + 1],
                                   accum_out=row_sum[:, slot, t:t + 1]).then_inc(exp_done, 1)

            def copy_probsT(b):
                act.wait_ge(probsT_done, b + 1)
                act.copy(probsT[:, :, :], probsT_ps[:, :].rearrange("p (k s) -> p k s", k=ST)).then_inc(probsT_copied, 1)

            def x1_high(b):
                act.wait_ge(x1_ready, b + 1)
                act.copy(x1hi[:, :, cols(b)], acc[:, :, cols(b)]).then_inc(x1hi_ready, 1)

            def gate(t, j):
                act.wait_ge(g_done, t + 1)
                act.activation(silu[j % 2][:, :], g_ps[j % 2][:, :], ACT.Silu).then_inc(silu_done, 1)

            def weights_high(f):
                (up_s, down_s), (up_d, down_d) = w_tile(up_in, down_in, f), w_tile(up_hi, down_hi, f)
                act.copy(up_d, up_s)
                act.copy(down_d, down_s).then_inc(w_hi_ready, 1)

            copy_x(0, 0)
            copy_k(0, 0)
            copy_x(1, 1)
            copy_k(1, 1)
            exponentials(0, 0)

            def attention(b, slot):
                copy_probsT(b - 1)
                copy_x(b + 1, 1 - slot)
                copy_k(b + 1, 1 - slot)
                exponentials(b, slot)

            attention(1, 1)
            x1_high(0)
            attention(2, 0)
            x1_high(1)
            with act.Fori(3, B - 2, 2) as b:
                for i in range(2):
                    attention(b + i, (1 + i) % 2)
                    if i == 0:
                        act.wait_ge(first_w_loaded, (b - 1) * (W_LOADS // 2))
                    weights_high(b + (i - 3))
                    x1_high(b + (i - 1))
            copy_probsT(B - 2)
            exponentials(B - 1, 1)
            x1_high(B - 2)
            act.wait_ge(first_w_loaded, 3 * W_LOADS)
            weights_high(4)
            copy_probsT(B - 1)
            gate(0, 0)
            weights_high(5)
            gate(1, 1)
            x1_high(B - 1)
            act.wait_ge(first_w_loaded, 4 * W_LOADS)
            weights_high(6)
            weights_high(7)

            with act.Fori(0, E) as e:
                for j in range(STEPS):
                    gate(e * STEPS + j + LAG, j + LAG)
                    if j == LAST:
                        act.wait_ge(w_loaded, (e + 1) * W_LOADS)
                    if j >= LAST:
                        act.wait_ge(down_done, e * STEPS + j + 1)
                        weights_high(j - LAST)
            for j in range(STEPS):
                if j + LAG < STEPS:
                    gate(E * STEPS + j + LAG, j + LAG)
                if j > FT and j % FT == LAG:
                    n = j // FT - 1
                    for half in range(2):
                        act.wait_ge(out_T_done, 2 * n + half + 1)
                        act.copy(y[2 * n + half][:, :, :],
                                 out_ps[n][half][:, :].rearrange("p (t d) -> p t d", t=2)).then_inc(y_ready, 1)
            for half in range(2):
                act.wait_ge(out_T_done, 2 * NB - 1 + half)
                act.copy(y[2 * NB - 2 + half][:, :, :],
                         out_ps[NB - 1][half][:, :].rearrange("p (t d) -> p t d", t=2)).then_inc(y_ready, 1)

        @block.vector
        def _(dve):
            def queries(b, slot):
                dve.wait_ge(xT_copied, b + 1)
                if isinstance(b, int) and b < 2:
                    dve.wait_ge(first_bias_loaded[b], 16)
                else:
                    dve.wait_ge(bias_loaded, 16 * (B - 2))
                dve.tensor_tensor(qT[slot][:, :, :], acc[:, :, cols(b)],
                                  bias[:, bass.ds(b, 1), :].broadcast_to([P, DT, S]), ALU.add).then_inc(q_ready, 1)

            def maxima(b, slot):
                dve.wait_ge(scores_done, b + 1)
                dve.tensor_reduce(neg_max[:, slot, :], s_ps[slot][:, :].rearrange("p (t s) -> p t s", t=ST),
                                  AX_X, ALU.max, negate=True).then_inc(max_ready, 1)

            def normalise(b, slot):
                for t in range(ST):
                    dve.wait_ge(exp_done, b * ST + t + 1)
                    dve.reciprocal(row_inv[:, slot, t:t + 1], row_sum[:, slot, t:t + 1]).then_inc(inv_ready, 1)
                    dve.wait_ge(inv_ready, b * ST + t + 1)
                    last = dve.tensor_scalar(probs[slot][:, t, :], probs[slot][:, t, :],
                                             row_inv[:, slot, t:t + 1], None, ALU.mult)
                last.then_inc(probs_ready, 1)

            def residual(b):
                dve.wait_ge(attn_done, b + 1)
                return dve.tensor_tensor(acc[:, :, cols(b)], attn_ps[:, :].rearrange("p (d s) -> p d s", d=DT),
                                         acc[:, :, cols(b)], ALU.add).then_inc(x1_ready, 1)

            def x1_low(b):
                dve.wait_ge(x1hi_ready, b + 1)
                dve.tensor_tensor(x1lo[:, :, cols(b)], acc[:, :, cols(b)], x1hi[:, :, cols(b)].bitcast(F32),
                                  ALU.subtract).then_inc(x1lo_ready, 1)

            def hidden(t, j):
                dve.wait_ge(silu_done, t + 1)
                dve.wait_ge(u_done, t + 1)
                dve.tensor_tensor(h[j % 2][:, :], u_ps[j % 2][:, :], silu[j % 2][:, :], ALU.mult).then_inc(h_done, 1)
                dve.wait_ge(h_done, t + 1)
                if j >= LAG:
                    dve.wait_ge(down_done, t - 1)
                dve.tensor_copy(h_hi[j % 2][:, :], h[j % 2][:, :]).then_inc(h_hi_ready, 1)
                dve.wait_ge(h_hi_ready, t + 1)
                dve.tensor_tensor(h_lo[j % 2][:, :], h[j % 2][:, :], h_hi[j % 2][:, :].bitcast(F32),
                                  ALU.subtract).then_inc(h_ready, 1)

            def take_block(e, n):
                dve.wait_ge(down_done, e * STEPS + (n + 1) * FT)
                for i in range(BPB):
                    b = BPB * n + i
                    for d in range(DT):
                        last = dve.scalar_tensor_tensor(acc[:, d, b * S:(b + 1) * S], down_ps[n % 2][d][:, i * S:(i + 1) * S],
                                                        coef[:, bass.ds(e * B + b, 1)], acc[:, d, b * S:(b + 1) * S],
                                                        ALU.mult, ALU.add)
                    last.then_inc(down_free, 1)

            def weights_low(e, f):
                dve.wait_ge(w_hi_ready, e * FT + f + 1)
                up_s, down_s = w_tile(up_in, down_in, f)
                up_h, down_h = w_tile(up_hi, down_hi, f)
                up_l, down_l = w_tile(up_lo, down_lo, f)
                dve.tensor_tensor(up_l, up_s, up_h.bitcast(F32), ALU.subtract)
                dve.tensor_tensor(down_l, down_s, down_h.bitcast(F32), ALU.subtract).then_inc(w_ready, 1)

            queries(0, 0)
            queries(1, 1)
            maxima(0, 0)
            normalise(0, 0)

            def attention(b, slot):
                maxima(b, slot)
                queries(b + 1, 1 - slot)
                normalise(b, slot)
                residual(b - 1)

            attention(1, 1)
            x1_low(0)
            attention(2, 0)
            x1_low(1)
            with dve.Fori(3, B - 2, 2) as b:
                for i in range(2):
                    attention(b + i, (1 + i) % 2)
                    weights_low(0, b + (i - 3))
                    x1_low(b + (i - 1))
            maxima(B - 1, 1)
            normalise(B - 1, 1)
            residual(B - 2)
            x1_low(B - 2)
            weights_low(0, 4)
            hidden(0, 0)
            residual(B - 1)
            dve.wait_ge(x1_ready, B)
            dve.tensor_copy(row_sum[:, 0, :], row_sum[:, 1, :]).then_inc(down_free, 2 * BPB)
            x1_low(B - 1)
            weights_low(0, 5)
            hidden(1, 1)
            weights_low(0, 6)
            weights_low(0, 7)
            dve.wait_ge(coef_ready, 2)

            with dve.Fori(0, E) as e:
                for j in range(STEPS):
                    hidden(e * STEPS + j + LAG, j + LAG)
                    if j >= LAST:
                        weights_low(e + 1, j - LAST)
                    if j % FT == FT - 1:
                        take_block(e, j // FT)
            for j in range(STEPS):
                if j + LAG < STEPS:
                    hidden(E * STEPS + j + LAG, j + LAG)
                if j % FT == FT - 1:
                    take_block(E, j // FT)

        @block.gpsimd
        def _(pool):
            pool.memset(ident[:, :], 0.0).then_inc(ident_zeroed, 1)
            pool.wait_ge(ident_zeroed, 1)
            pool.affine_select(out=ident[:, :], in_=ident[:, :], compare_op=ALU.not_equal, fill=1.0, base=0,
                               pattern=[[-1, P]], channel_multiplier=1).then_inc(ident_ready, 1)

            pool.wait_ge(stage_loaded, 16)
            for b in range(2, B):
                load_bias(pool, b).then_inc(bias_loaded, 16)
            pool.dma_start(gate_bc[:, :], gating.rearrange("(o b) e -> o (b e)", o=1).partition_broadcast(P)).then_inc(gates_loaded, 16)
            pool.dma_start(shared_bc[:, :], shared_gate.rearrange("(o b) -> o b", o=1).partition_broadcast(P)).then_inc(gates_loaded, 16)

            pool.wait_ge(gates_loaded, 32)
            pool.tensor_scalar(unshared[:, :], shared_bc[:, :], -1.0, 1.0, ALU.mult, ALU.add).then_inc(unshared_ready, 1)
            pool.tensor_copy(coef[:, E * B:(E + 1) * B], shared_bc[:, :]).then_inc(coef_ready, 1)
            pool.wait_ge(unshared_ready, 1)
            pool.tensor_tensor(coef[:, 0:E * B].rearrange("p (e b) -> p e b", e=E),
                               gate_bc[:, :].rearrange("p (b e) -> p e b", b=B),
                               unshared[:, :].rearrange("p (o b) -> p o b", o=1).broadcast_to([P, E, B]),
                               ALU.mult).then_inc(coef_ready, 1)


_INS = ["x", "fside_BxSxS_0", "itok_B_0_5", "fside_Bx8_0", "condB_sharedgateprob", "L0_cond_braak_embed",
        "L1_cond_Wg", "L1_cond_Wu", "L1_cond_Wd", "L1_cond_Sg", "L1_cond_Su", "L1_cond_Sd"]


def kernel(**inputs):
    import numpy as np
    import concourse.bacc as bacc
    from concourse.bass_utils import run_bass_kernel_spmd

    nc = bacc.Bacc("TRN2", target_bir_lowering=False, num_devices=1)
    arrays, args = {}, []
    for name in _INS:
        a = np.ascontiguousarray(inputs[name])
        arrays[f"in_{name}"] = a
        args.append(nc.dram_tensor(f"in_{name}", a.shape, mybir.dt.from_np(a.dtype), kind="ExternalInput").ap())
    out = nc.dram_tensor("out", inputs["x"].shape, F32, kind="ExternalOutput").ap()
    build(nc, *args, out)
    r = run_bass_kernel_spmd(nc, [arrays], core_ids=[0])
    return r.results[0]["out"]
```
